# Optimizing a Trainium2 kernel written in Bass

```python
import numpy as np
import jax
import jax.numpy as jnp

def _softmax(x, axis=-1):
    return jax.nn.softmax(x, axis=axis)

def _gelu(x):
    return jax.nn.gelu(x, approximate=True)

def _silu(x):
    return jax.nn.silu(x)

def _sigmoid(x):
    return jax.nn.sigmoid(x)

def _layernorm(x, axis=-1, eps=1e-05):
    m = jnp.mean(x, axis=axis, keepdims=True)
    v = jnp.var(x, axis=axis, keepdims=True)
    return (x - m) / jnp.sqrt(v + eps)

def _scatter_add(tgt, idx, src, axis=0):
    return tgt.at[idx].add(src)

def _segment_sum(src, seg, n):
    return jax.ops.segment_sum(src, seg, n)
kernel_name = 'mk_gnn_resnorm_d2_gnn_r8_fbbfc9'

def setup_inputs(seed: int=0):
    np.random.seed(seed)
    _w = jnp.asarray

    def _rec_inputs():
        import jax
        import jax.numpy as jnp
        _gk = jax.random.key(seed)
        x = -0.0003713 + 1 * jax.random.normal(jax.random.fold_in(_gk, 1), (12500, 256), jnp.float32)
        src = jax.random.randint(jax.random.fold_in(_gk, 2), (200000,), 0, 12500, jnp.int32)
        dst = jax.random.randint(jax.random.fold_in(_gk, 3), (200000,), 0, 12500, jnp.int32)
        _o = jnp.argsort(dst, stable=True)
        src = src[_o]
        dst = dst[_o]
        edge_attr_3 = 0.000669165 + 0.999965 * jax.random.normal(jax.random.fold_in(_gk, 11), (200000, 3), jnp.float32)
        edge_type_64 = jax.random.randint(jax.random.fold_in(_gk, 13), (200000,), 0, 64, jnp.int32)
        return (x, src, dst, edge_attr_3, edge_type_64)
    x, src, dst, edge_attr_3, edge_type_64 = _rec_inputs()

    def _L0_gnn_setup():
        import jax, jax.numpy as jnp
        import numpy as np
        N_NODES = 6250
        N_EDGES = 62500
        IN_DIM = 256
        HID = 64
        HEADS = 4
        N_REL = 64
        key = jax.random.key(seed)
        ks = jax.random.split(key, 16)
        s = 0.02
        return {'node_features': jax.random.normal(ks[0], (N_NODES, IN_DIM), jnp.float32), 'edge_index': jax.random.randint(ks[1], (2, N_EDGES), 0, N_NODES, jnp.int32), 'edge_relations': jax.random.randint(ks[2], (N_EDGES,), 0, N_REL, jnp.int32), 'query_emb': jax.random.normal(ks[3], (IN_DIM,), jnp.float32), 'Wq': jax.random.normal(ks[4], (IN_DIM, HID * HEADS), jnp.float32) * s, 'bq': jnp.zeros((HID * HEADS,), jnp.float32), 'Wk': jax.random.normal(ks[5], (IN_DIM, HID * HEADS), jnp.float32) * s, 'bk': jnp.zeros((HID * HEADS,), jnp.float32), 'Wv': jax.random.normal(ks[6], (IN_DIM, HID * HEADS), jnp.float32) * s, 'bv': jnp.zeros((HID * HEADS,), jnp.float32), 'rel_w': jax.random.normal(ks[7], (N_REL, HID), jnp.float32) * s, 'Wo': jax.random.normal(ks[8], (HID * HEADS, IN_DIM), jnp.float32) * s, 'bo': jnp.zeros((IN_DIM,), jnp.float32), 'gamma': jnp.ones((IN_DIM,), jnp.float32), 'beta': jnp.zeros((IN_DIM,), jnp.float32)}
    _L0_gnn_all = _L0_gnn_setup()
    _L0_gnn_in = {k: v for k, v in _L0_gnn_all.items() if k in ('query_emb', 'Wq', 'bq', 'Wk', 'bk', 'Wv', 'bv', 'rel_w', 'Wo', 'bo', 'gamma', 'beta')}
    del _L0_gnn_all

    def _L1_gnn_setup():
        import jax, jax.numpy as jnp
        import numpy as np
        N = 6250
        H = 256
        E = 100000
        F = 3
        DIST_SCALE = 4.0
        LN_EPS = 1e-05
        key = jax.random.key(seed)
        ks = jax.random.split(key, 8)
        x = jax.random.normal(ks[0], (N, H), dtype=jnp.float32)
        edge_index = jax.random.randint(ks[1], (2, E), 0, N, dtype=jnp.int64)
        edge_attr = jax.random.normal(ks[2], (E, F), dtype=jnp.float32)
        W1 = jax.random.normal(ks[3], (H, H), dtype=jnp.float32) * 0.02
        b1 = jnp.zeros((H,), dtype=jnp.float32)
        W2 = jax.random.normal(ks[4], (H, H), dtype=jnp.float32) * 0.02
        b2 = jnp.zeros((H,), dtype=jnp.float32)
        gamma = jnp.ones((H,), dtype=jnp.float32)
        beta = jnp.zeros((H,), dtype=jnp.float32)
        return {'x': x, 'edge_index': edge_index, 'edge_attr': edge_attr, 'W1': W1, 'b1': b1, 'W2': W2, 'b2': b2, 'gamma': gamma, 'beta': beta}
    _L1_gnn_all = _L1_gnn_setup()
    _L1_gnn_in = {k: v for k, v in _L1_gnn_all.items() if k in ('W1', 'b1', 'W2', 'b2', 'gamma', 'beta')}
    del _L1_gnn_all
    return {'x': x, 'src': src, 'dst': dst, 'edge_attr_3': edge_attr_3, 'edge_type_64': edge_type_64, 'L0_gnn_query_emb': _L0_gnn_in['query_emb'], 'L0_gnn_Wq': _L0_gnn_in['Wq'], 'L0_gnn_bq': _L0_gnn_in['bq'], 'L0_gnn_Wk': _L0_gnn_in['Wk'], 'L0_gnn_bk': _L0_gnn_in['bk'], 'L0_gnn_Wv': _L0_gnn_in['Wv'], 'L0_gnn_bv': _L0_gnn_in['bv'], 'L0_gnn_rel_w': _L0_gnn_in['rel_w'], 'L0_gnn_Wo': _L0_gnn_in['Wo'], 'L0_gnn_bo': _L0_gnn_in['bo'], 'L0_gnn_gamma': _L0_gnn_in['gamma'], 'L0_gnn_beta': _L0_gnn_in['beta'], 'L1_gnn_W1': _L1_gnn_in['W1'], 'L1_gnn_b1': _L1_gnn_in['b1'], 'L1_gnn_W2': _L1_gnn_in['W2'], 'L1_gnn_b2': _L1_gnn_in['b2'], 'L1_gnn_gamma': _L1_gnn_in['gamma'], 'L1_gnn_beta': _L1_gnn_in['beta']}

def reference(x, src, dst, edge_attr_3, edge_type_64, L0_gnn_query_emb, L0_gnn_Wq, L0_gnn_bq, L0_gnn_Wk, L0_gnn_bk, L0_gnn_Wv, L0_gnn_bv, L0_gnn_rel_w, L0_gnn_Wo, L0_gnn_bo, L0_gnn_gamma, L0_gnn_beta, L1_gnn_W1, L1_gnn_b1, L1_gnn_W2, L1_gnn_b2, L1_gnn_gamma, L1_gnn_beta):
    import jax
    import jax.numpy as jnp

    def _L0_gnn_ref(node_features, edge_index, edge_relations, query_emb, Wq, bq, Wk, bk, Wv, bv, rel_w, Wo, bo, gamma, beta):
        import jax, jax.numpy as jnp
        import numpy as np
        N_NODES = 6250
        N_EDGES = 62500
        IN_DIM = 256
        HID = 64
        HEADS = 4
        N_REL = 64
        N = node_features.shape[0]
        D = rel_w.shape[1]
        H = Wq.shape[1] // D
        enh = node_features + 0.1 * query_emb[None, :]
        Q = (enh @ Wq + bq).reshape(N, H, D)
        K = (enh @ Wk + bk).reshape(N, H, D)
        V = (enh @ Wv + bv).reshape(N, H, D)
        src, dst = (edge_index[0], edge_index[1])
        rel = rel_w[edge_relations]
        mod_k = K[src] + 0.2 * rel[:, None, :]
        scores = jnp.einsum('ehd,ehd->eh', Q[dst], mod_k) / D ** 0.5
        seg_max = jax.ops.segment_max(scores, dst, num_segments=N)
        ex = jnp.exp(scores - seg_max[dst])
        denom = jax.ops.segment_sum(ex, dst, num_segments=N)
        w = ex / denom[dst]
        agg = jax.ops.segment_sum(w[:, :, None] * V[src], dst, num_segments=N)
        deg = jax.ops.segment_sum(jnp.ones((src.shape[0],), jnp.float32), dst, num_segments=N)
        msgs = jnp.where(deg[:, None, None] > 0, agg, V)
        out = msgs.reshape(N, H * D) @ Wo + bo
        x = out + node_features
        mu = jnp.mean(x, axis=-1, keepdims=True)
        var = jnp.var(x, axis=-1, keepdims=True)
        return (x - mu) / jnp.sqrt(var + 1e-05) * gamma + beta

    def _L1_gnn_ref(x, edge_index, edge_attr, W1, b1, W2, b2, gamma, beta):
        import jax, jax.numpy as jnp
        import numpy as np
        N = 6250
        H = 256
        E = 100000
        F = 3
        DIST_SCALE = 4.0
        LN_EPS = 1e-05
        src = edge_index[0]
        dst = edge_index[1]
        n_nodes = x.shape[0]
        feat = edge_attr.astype(jnp.float32)
        feat_norm = jnp.sqrt(jnp.sum(feat * feat, axis=1) + 1e-12)
        w = jnp.exp(-DIST_SCALE * feat_norm).astype(x.dtype)
        w = jnp.maximum(w, 0.0)
        weighted = x[src] * w[:, None]
        agg = jax.ops.segment_sum(weighted, dst, num_segments=n_nodes)
        wsum = jax.ops.segment_sum(w, dst, num_segments=n_nodes)
        agg = agg / jnp.maximum(wsum, 1e-06)[:, None]
        h = jax.nn.gelu(jnp.dot(agg, W1.T) + b1, approximate=False)
        msg = jnp.dot(h, W2.T) + b2
        y = x + msg
        mu = jnp.mean(y, axis=-1, keepdims=True)
        var = jnp.mean(jnp.square(y - mu), axis=-1, keepdims=True)
        return (y - mu) * jax.lax.rsqrt(var + LN_EPS) * gamma + beta
    edge_index = jnp.stack([src, dst])
    x = _layernorm(x + _L0_gnn_ref(x, edge_index, edge_type_64, L0_gnn_query_emb, L0_gnn_Wq, L0_gnn_bq, L0_gnn_Wk, L0_gnn_bk, L0_gnn_Wv, L0_gnn_bv, L0_gnn_rel_w, L0_gnn_Wo, L0_gnn_bo, L0_gnn_gamma, L0_gnn_beta), axis=-1)
    x = _layernorm(x + _L1_gnn_ref(x, edge_index, edge_attr_3, L1_gnn_W1, L1_gnn_b1, L1_gnn_W2, L1_gnn_b2, L1_gnn_gamma, L1_gnn_beta), axis=-1)
    return x

_drawn_inputs = setup_inputs


def setup_inputs(seed=0):
    import zlib

    import numpy as np

    out = dict(_drawn_inputs(seed))
    spreads = {'L0_gnn_bq': (0.0, 0.8),
     'L0_gnn_bk': (0.0, 2.0),
     'L0_gnn_bv': (0.0, 0.509),
     'L0_gnn_bo': (0.0, 0.1),
     'L0_gnn_gamma': (1.0, 0.2),
     'L0_gnn_beta': (0.0, 0.1),
     'L1_gnn_b1': (0.0, 0.8),
     'L1_gnn_b2': (0.0, 0.1),
     'L1_gnn_gamma': (1.0, 0.2),
     'L1_gnn_beta': (0.0, 0.1)}
    factors = {'edge_attr_3': 4.128,
     'L0_gnn_query_emb': 8.0,
     'L0_gnn_Wq': 8.0,
     'L0_gnn_Wk': 8.0,
     'L0_gnn_Wv': 3.999,
     'L0_gnn_rel_w': 47.702,
     'L0_gnn_Wo': 2.698,
     'L1_gnn_W1': 3.635,
     'L1_gnn_W2': 3.223}
    for name, (base, spread) in spreads.items():
        noise = np.random.default_rng([zlib.crc32(name.encode()), seed]).standard_normal(out[name].shape)
        drawn = base * np.exp(spread * noise) if base else spread * noise
        out[name] = jnp.asarray(drawn.astype(out[name].dtype))
    for name, factor in factors.items():
        out[name] = (out[name] * factor).astype(out[name].dtype)
    return out
```

```python
from contextlib import ExitStack

import concourse.bass as bass
from concourse import mybir

F32 = mybir.dt.float32
BF16 = mybir.dt.bfloat16
I32 = mybir.dt.int32
ALU = mybir.AluOpType
ACT = mybir.ActivationFunctionType
AX = mybir.AxisListType
ENGINE = mybir.EngineType

P = 128
N = 12500
E = 200000
D = 256
HEADS = 4
HD = D // HEADS
REL = 64
FC = D // P
NODE_TILES = -(-N // P)
NPAD = NODE_TILES * P
LAST_ROWS = N - (NODE_TILES - 1) * P
EDGE_TILES = -(-E // P)
GROUPS = -(-(EDGE_TILES + NODE_TILES - 1) // P)
STEPS = GROUPS * P
SLOTS = GROUPS * P
FULL_ROWS = E // SLOTS
TAIL = E - FULL_ROWS * SLOTS
FIELDS = 4
BODY = 16
HALF = BODY // 2
ITERS = STEPS // BODY
BATCH = 7
BATCHES = NODE_TILES // BATCH
PAIRS = BATCHES // 2
ACCW = D + HEADS
PAD_DST = 30000.0
NEG = -1.0e30
EPS = 1e-5
SCALE = HD ** -0.5
assert NODE_TILES == BATCH * BATCHES and BATCHES == 2 * PAIRS and STEPS == ITERS * BODY
assert EDGE_TILES <= STEPS and STEPS % GROUPS == 0


class Chain:

    def __init__(self, engine, sem):
        self.engine, self.sem, self.n = engine, sem, 0

    def after(self, op):
        self.n += 1
        op.then_inc(self.sem, 1)
        self.engine.wait_ge(self.sem, self.n)


def gnn_kernel(nc, x, src, dst, edge_attr, edge_type, query, wq, bq, wk, bk, wv, bv, rel_w, wo, bo, gamma0, beta0,
               w1, b1, w2, b2, gamma1, beta1, out):
    top = ExitStack()

    def sem(name):
        return top.enter_context(nc.semaphore(name))

    def tile(ctx, name, shape, dt=F32):
        return ctx.enter_context(nc.sbuf_tensor(name, shape, dt))

    def bank(ctx, name, shape, dt=F32):
        return ctx.enter_context(nc.psum_tensor(name, shape, dt))

    def carve(flat, shape, dt=F32, at=[0], start=None):
        if start is not None:
            at[0] = start
        n = 1
        for m in shape[1:]:
            n *= m
        words = n if dt != BF16 else n // 2
        assert at[0] + words <= flat.shape[1]
        part = flat[:, at[0]:at[0] + words]
        at[0] += words
        part = part if dt == F32 else part.bitcast(dt)
        names = "abcd"[:len(shape) - 1]
        if len(shape) > 2:
            part = part.rearrange(f"p ({' '.join(names)}) -> p {' '.join(names)}", **dict(zip(names, shape[1:])))
        return part

    def row(vector):
        return vector.rearrange("(a n) -> a n", a=1)

    rec_d = nc.dram_tensor("edge_records", [STEPS, FIELDS * P], F32).ap()
    match_d = nc.dram_tensor("match_rows", [STEPS, 2 * P], BF16).ap()
    k_d = nc.dram_tensor("k_rows", [NPAD, D], F32).ap()
    v_d = nc.dram_tensor("v_rows", [NPAD, D], F32).ap()
    x1_d = nc.dram_tensor("x1_rows", [NPAD, D], F32).ap()

    with top:
        node_acc = tile(top, "node_acc", [P, NODE_TILES, ACCW])
        scores = tile(top, "scores", [P, STEPS, HEADS])
        src_idx = tile(top, "src_idx", [P, STEPS], I32)
        dst_rel = tile(top, "dst_rel", [P, STEPS])
        dist_w = tile(top, "dist_w", [P, STEPS])
        step_node = tile(top, "step_node", [1, STEPS], I32)
        acc_flat = node_acc[:].rearrange("p j n -> p (j n)")
        flags = tile(top, "flags", [P, 2, SLOTS])
        flags_flat = flags[:].rearrange("p a n -> p (a n)")
        same_prev = flags[:, 0]
        same_next = flags[:, 1]
        carry_fw = tile(top, "carry_fw", [P, 1])
        carry_bw = tile(top, "carry_bw", [P, 1])
        col_id = tile(top, "col_id", [P, P])
        row_id = tile(top, "row_id", [P, 1])
        neg_row_id = tile(top, "neg_row_id", [P, 1])
        ident = tile(top, "ident", [P, P])
        ones_row = tile(top, "ones_row", [1, P])
        zero_col = tile(top, "zero_col", [P, 1])
        idx_now = tile(top, "idx_now", [P, 2, HALF], I32)
        ring = tile(top, "ring", [P, BODY, D + 1])

        scores_flat = scores[:].rearrange("p s h -> p (s h)")
        ring_flat = ring[:].rearrange("p u n -> p (u n)")
        gathered = [sem(f"gathered{u}") for u in range(BODY)]
        idx_landed = [sem("idx_landed0"), sem("idx_landed1")]
        half_begun = sem("half_begun")
        c_dve = sem("c_dve")
        dve_total = [0]

        def chain(engine, s, total):
            c = Chain(engine, s)
            c.n = total[0]
            return c

        with ExitStack() as ctx:
            src_i = carve(acc_flat, [P, SLOTS], I32, start=0)
            dst_i = carve(acc_flat, [P, SLOTS], I32)
            typ_i = carve(acc_flat, [P, SLOTS], I32)
            attr = carve(acc_flat, [P, 3 * SLOTS])
            rec = carve(acc_flat, [P, GROUPS, FIELDS, P])
            norm = carve(acc_flat, [P, SLOTS])
            before = carve(acc_flat, [P, P, GROUPS])
            step_id = carve(acc_flat, [P, STEPS])
            started = carve(acc_flat, [P, STEPS])
            rows = scores[:].rearrange("p s h -> p (s h)").rearrange("p (g f n) -> p g f n", g=GROUPS, n=P)
            tiles_before = tile(ctx, "tiles_before", [P, P])
            node_lo = tile(ctx, "node_lo", [P, P])
            node_lo_col = tile(ctx, "node_lo_col", [P, 1])
            col_id_1 = tile(ctx, "col_id_1", [P, P])
            next_m = tile(ctx, "next_m", [P, P])
            prev_m = tile(ctx, "prev_m", [P, P])
            below_m = tile(ctx, "below_m", [P, P])
            ones = tile(ctx, "ones", [P, P])
            cut = tile(ctx, "cut", [P, FIELDS * P])
            cut_lt = tile(ctx, "cut_lt", [P, P])
            cnt_i = tile(ctx, "cnt_i", [P, 1], I32)
            tab = tile(ctx, "tab", [P, 16])
            pair = tile(ctx, "pair", [P, 2])
            step_q = tile(ctx, "step_q", [P, GROUPS])
            jt = tile(ctx, "jt", [P, GROUPS, 2])
            tile_f = tile(ctx, "tile_f", [P, GROUPS])
            tile_i = tile(ctx, "tile_i", [P, GROUPS], I32)
            ps = bank(ctx, "ps_tab", [P, 16])
            ps_jt = bank(ctx, "ps_jt", [P, GROUPS, 2])
            ps_row = bank(ctx, "ps_row", [1, 4, 512])
            raw_ready, padded, consts, rec_ready, rec_stored = (
                sem("raw_ready"), sem("padded"), sem("consts"), sem("rec_ready"), sem("rec_stored"))
            sq_ready, norm_ready, cnt_ready, cut_ready, pe_done, dve_asks = (
                sem("sq_ready"), sem("norm_ready"), sem("cnt_ready"), sem("cut_ready"), sem("pe_done"), sem("dve_asks"))
            rows_ready = sem("rows_ready")

            with nc.Block() as block:

                @block.sync
                def _(sp):
                    sp.wait_ge(padded, 4)
                    for buf, vec, w in ((src_i, src, 1), (dst_i, dst, 1), (typ_i, edge_type, 1)):
                        sp.dma_start(buf[0:FULL_ROWS, :], vec[0:FULL_ROWS * SLOTS].rearrange(
                            "(p n) -> p n", p=FULL_ROWS)).then_inc(raw_ready, 16)
                        sp.dma_start(buf[FULL_ROWS:FULL_ROWS + 1, 0:TAIL], row(vec[FULL_ROWS * SLOTS:E])).then_inc(raw_ready, 16)
                    flat = edge_attr.rearrange("e c -> (e c)")
                    sp.dma_start(attr[0:FULL_ROWS, :], flat[0:FULL_ROWS * SLOTS * 3].rearrange(
                        "(p n) -> p n", p=FULL_ROWS)).then_inc(raw_ready, 16)
                    sp.dma_start(attr[FULL_ROWS:FULL_ROWS + 1, 0:3 * TAIL], row(flat[FULL_ROWS * SLOTS * 3:3 * E])).then_inc(raw_ready, 16)
                    sp.wait_ge(rec_ready, 1)
                    sp.dma_start(rec_d.rearrange("(p g) n -> p g n", g=GROUPS),
                                 rec[:].rearrange("p g f n -> p g (f n)")).then_inc(rec_stored, 16)
                    sp.wait_ge(rec_stored, 16)

                @block.gpsimd
                def _(pool):
                    iota = dict(allow_small_or_imprecise_dtypes=True)
                    nc.gpsimd.iota(col_id[:], [[1, P]], base=0, channel_multiplier=0, **iota).then_inc(consts, 1)
                    nc.gpsimd.iota(row_id[:], [[0, 1]], base=0, channel_multiplier=1, **iota).then_inc(consts, 1)
                    nc.gpsimd.iota(neg_row_id[:], [[0, 1]], base=0, channel_multiplier=-1, **iota).then_inc(consts, 1)
                    nc.gpsimd.iota(node_lo[:], [[P, P]], base=0, channel_multiplier=0, **iota).then_inc(consts, 1)
                    nc.gpsimd.iota(node_lo_col[:], [[0, 1]], base=0, channel_multiplier=P, **iota).then_inc(consts, 1)
                    nc.gpsimd.iota(col_id_1[:], [[1, P]], base=1, channel_multiplier=0, **iota).then_inc(consts, 1)
                    nc.gpsimd.iota(step_id[:], [[1, STEPS]], base=0, channel_multiplier=0, **iota).then_inc(consts, 1)
                    nc.gpsimd.iota(step_q[:], [[1, GROUPS]], base=0, channel_multiplier=GROUPS, **iota).then_inc(consts, 1)
                    pool.wait_ge(rec_stored, 16)
                    pool.wait_ge(cnt_ready, 1)
                    nc.gpsimd.indirect_dma_start(out=cut[:], out_offset=None, in_=rec_d, in_offset=bass.IndirectOffsetOnAxis(
                        ap=cnt_i[:], axis=0)).then_inc(cut_ready, 16)
                    pool.wait_ge(cnt_ready, 2)
                    for g in range(GROUPS):
                        nc.gpsimd.indirect_dma_start(
                            out=rows[:, g].rearrange("p f n -> p (f n)"), out_offset=None, in_=rec_d,
                            in_offset=bass.IndirectOffsetOnAxis(ap=tile_i[:, g:g + 1], axis=0)).then_inc(rows_ready, 16)
                    pool.wait_ge(rows_ready, 16 * GROUPS)

                @block.scalar
                def _(act):
                    act.wait_ge(sq_ready, 1)
                    nc.scalar.activation(norm[:], norm[:], ACT.Sqrt).then_inc(norm_ready, 1)
                    act.wait_ge(norm_ready, 1)
                    nc.scalar.activation(norm[:], norm[:], ACT.Exp, scale=-4.0).then_inc(norm_ready, 1)

                @block.vector
                def _(v):
                    ch = chain(v, c_dve, dve_total)
                    nc.vector.memset(src_i[96:P, :], 0).then_inc(padded, 1)
                    nc.vector.memset(dst_i[96:P, :], int(PAD_DST)).then_inc(padded, 1)
                    nc.vector.memset(typ_i[96:P, :], 0).then_inc(padded, 1)
                    nc.vector.memset(attr[96:P, :], 0.0).then_inc(padded, 1)
                    nc.vector.memset(ones[:], 1.0)
                    nc.vector.memset(ones_row[:], 1.0)
                    nc.vector.memset(zero_col[:], 0.0)
                    v.wait_ge(consts, 8)
                    nc.vector.tensor_scalar(ident[:], col_id[:], row_id[:, 0:1], None, ALU.is_equal)
                    nc.vector.tensor_scalar(next_m[:], col_id_1[:], row_id[:, 0:1], None, ALU.is_equal)
                    nc.vector.tensor_scalar(prev_m[:], col_id[:], 1.0, row_id[:, 0:1], ALU.subtract, ALU.is_equal)
                    nc.vector.tensor_scalar(below_m[:], col_id[:], row_id[:, 0:1], None, ALU.is_gt)
                    v.wait_ge(raw_ready, 8 * 16)
                    field = [rec[:, :, f, :] for f in range(FIELDS)]
                    for f, buf in enumerate((src_i, dst_i, typ_i)):
                        ch.after(nc.vector.tensor_copy(field[f], buf[:].rearrange("p (g n) -> p g n", n=P)))
                    ch.after(nc.vector.tensor_tensor(attr[:], attr[:], attr[:], ALU.mult))
                    ch.after(nc.vector.tensor_reduce(norm[:], attr[:].rearrange("p (n c) -> p n c", c=3), AX.X, ALU.add))
                    nc.vector.tensor_scalar(norm[:], norm[:], 1e-12, None, ALU.add).then_inc(sq_ready, 1)
                    ch.after(nc.vector.tensor_tensor(
                        before[:], rec[:, :, 1, P - 1].unsqueeze(1).to_broadcast([P, P, GROUPS]),
                        node_lo[:].unsqueeze(2).to_broadcast([P, P, GROUPS]), ALU.is_lt))
                    ch.after(nc.vector.tensor_reduce(tiles_before[:], before[:], AX.X, ALU.add))
                    v.sem_inc(dve_asks, 1)
                    v.wait_ge(norm_ready, 2)
                    nc.vector.tensor_scalar(field[3], norm[:].rearrange("p (g n) -> p g n", n=P), 0.0, None, ALU.max).then_inc(rec_ready, 1)
                    v.wait_ge(pe_done, 1)
                    ch.after(nc.vector.tensor_copy(tab[:, 1:2], ps[:, 0:1]))
                    nc.vector.tensor_copy(cnt_i[:], tab[:, 1:2]).then_inc(cnt_ready, 1)
                    v.wait_ge(cut_ready, 16)
                    ch.after(nc.vector.tensor_scalar(cut_lt[:], cut[:, P:2 * P], node_lo_col[:, 0:1], None, ALU.is_lt))
                    ch.after(nc.vector.tensor_reduce(tab[:, 3:4], cut_lt[:], AX.X, ALU.add))
                    ch.after(nc.vector.scalar_tensor_tensor(out=tab[:, 0:1], in0=tab[:, 1:2], scalar=float(P),
                                                            in1=tab[:, 3:4], op0=ALU.mult, op1=ALU.add))
                    ch.after(nc.vector.scalar_tensor_tensor(out=tab[:, 2:3], in0=tab[:, 3:4], scalar=0.0,
                                                            in1=tab[:, 1:2], op0=ALU.is_gt, op1=ALU.add))
                    v.sem_inc(dve_asks, 1)
                    v.wait_ge(pe_done, 2)
                    ch.after(nc.vector.tensor_tensor(tab[:, 4:5], ps[:, 3:4], tab[:, 1:2], ALU.subtract))
                    ch.after(nc.vector.tensor_tensor(tab[:, 5:6], ps[:, 1:2], tab[:, 0:1], ALU.is_gt))
                    ch.after(nc.vector.tensor_tensor(tab[:, 6:7], tab[:, 4:5], tab[:, 5:6], ALU.mult))
                    v.sem_inc(dve_asks, 1)
                    v.wait_ge(pe_done, 3)
                    ch.after(nc.vector.tensor_tensor(tab[:, 7:8], ps[:, 4:5], tab[:, 6:7], ALU.add))
                    ch.after(nc.vector.tensor_tensor(tab[:, 8:9], tab[:, 1:2], ps[:, 4:5], ALU.subtract))
                    v.sem_inc(dve_asks, 1)
                    ch.after(nc.vector.tensor_scalar(started[:], step_id[:], tab[:, 7:8], None, ALU.is_ge))
                    ch.after(nc.vector.memset(pair[:, 0:1], 1.0))
                    v.wait_ge(pe_done, 4)
                    ch.after(nc.vector.tensor_tensor(pair[:, 1:2], ps[:, 5:6], tab[:, 8:9], ALU.subtract))
                    v.sem_inc(dve_asks, 1)
                    v.wait_ge(pe_done, 5)
                    ch.after(nc.vector.tensor_copy(jt[:], ps_jt[:]))
                    ch.after(nc.vector.tensor_tensor(tile_f[:], jt[:, :, 1], step_q[:], ALU.add))
                    nc.vector.tensor_scalar(tile_i[:], tile_f[:], 0.0, float(STEPS - 1), ALU.max, ALU.min).then_inc(cnt_ready, 1)
                    for c in range(4):
                        w = STEPS // 4
                        nc.vector.tensor_scalar(step_node[0:1, c * w:(c + 1) * w], ps_row[0:1, c, 0:w],
                                                float(NODE_TILES - 1), None, ALU.min)
                    dve_total[0] = ch.n

                @block.tensor
                def _(pe):
                    pe.wait_ge(dve_asks, 1)
                    nc.tensor.matmul(ps[:, 0:1], tiles_before[:], ones[:, 0:1], start=True, stop=True).then_inc(pe_done, 1)
                    pe.wait_ge(dve_asks, 2)
                    nc.tensor.matmul(ps[:, 1:4], next_m[:], tab[:, 0:3], start=True, stop=True).then_inc(pe_done, 1)
                    pe.wait_ge(dve_asks, 3)
                    nc.tensor.matmul(ps[:, 4:5], below_m[:], tab[:, 6:7], start=True, stop=True).then_inc(pe_done, 1)
                    pe.wait_ge(dve_asks, 4)
                    nc.tensor.matmul(ps[:, 5:6], next_m[:], tab[:, 8:9], start=True, stop=True).then_inc(pe_done, 1)
                    pe.wait_ge(dve_asks, 5)
                    steps = started[:].rearrange("p (q g) -> p g q", g=GROUPS)
                    for g in range(GROUPS):
                        nc.tensor.matmul(ps_jt[:, g, :], steps[:, g, :], pair[:], start=True, stop=True)
                    for c in range(4):
                        w = STEPS // 4
                        last = nc.tensor.matmul(ps_row[0:1, c, 0:w], ones[:, 0:1], started[:, c * w:(c + 1) * w], start=True, stop=True)
                    last.then_inc(pe_done, 1)

            with ExitStack() as sub:
                rel_row = carve(acc_flat, [P, GROUPS, P], start=0)
                valid = carve(acc_flat, [P, GROUPS, P])
                match = carve(acc_flat, [P, GROUPS, 2, P], BF16)
                key = carve(acc_flat, [P, SLOTS + 2])
                ps_t = bank(sub, "ps_t", [P, 2, 4, P])
                match_ready, match_stored, rel_ready, key_ready, moved, turned, taken = (
                    sem("match_ready"), sem("match_stored"), sem("rel_ready"), sem("key_ready"), sem("moved"),
                    sem("turned"), sem("taken"))
                with nc.Block() as block:

                    @block.sync
                    def _(sp):
                        sp.wait_ge(match_ready, 2)
                        sp.dma_start(match_d.rearrange("(p g) n -> p g n", g=GROUPS),
                                     match[:].rearrange("p g f n -> p g (f n)")).then_inc(match_stored, 16)
                        sp.wait_ge(match_stored, 16)

                    @block.vector
                    def _(v):
                        ch = chain(v, c_dve, dve_total)
                        ch.after(nc.vector.tensor_scalar(tile_f[:], jt[:, :, 0], -float(P), None, ALU.mult))
                        nc.vector.tensor_tensor(rel_row[:], rows[:, :, 1, :], tile_f[:].unsqueeze(2).to_broadcast([P, GROUPS, P]),
                                                ALU.add).then_inc(rel_ready, 1)
                        v.wait_ge(rel_ready, 1)
                        nc.vector.tensor_copy(match[:, :, 0, :], rel_row[:]).then_inc(match_ready, 1)
                        nc.vector.tensor_copy(match[:, :, 1, :], rows[:, :, 2, :]).then_inc(match_ready, 1)
                        ch.after(nc.vector.tensor_scalar(valid[:], rel_row[:], float(P - 1), None, ALU.is_le))
                        ch.after(nc.vector.scalar_tensor_tensor(out=valid[:].rearrange("p g n -> p (g n)"), in0=rel_row[:].rearrange("p g n -> p (g n)"), scalar=0.0,
                                                                in1=valid[:].rearrange("p g n -> p (g n)"), op0=ALU.is_ge, op1=ALU.mult))
                        ch.after(nc.vector.tensor_scalar(rows[:, :, 1, :], rows[:, :, 1, :], 1.0, None, ALU.add))
                        ch.after(nc.vector.tensor_tensor(key[:, 1:SLOTS + 1].rearrange("p (g n) -> p g n", n=P), rows[:, :, 1, :], valid[:], ALU.mult))
                        v.sem_inc(key_ready, 1)
                        v.wait_ge(moved, 1)
                        ch.after(nc.vector.tensor_copy(key[:, 0:1], ps[:, 8:9]))
                        ch.after(nc.vector.tensor_copy(key[:, SLOTS + 1:SLOTS + 2], ps[:, 9:10]))
                        own = key[:, 1:SLOTS + 1]
                        for flag, a, b in ((same_prev, own, key[:, 0:SLOTS]), (same_next, own, key[:, 2:SLOTS + 2]),
                                           (carry_fw[:], key[:, SLOTS:SLOTS + 1], key[:, 0:1]),
                                           (carry_bw[:], key[:, 1:2], key[:, SLOTS + 1:SLOTS + 2])):
                            ch.after(nc.vector.tensor_tensor(flag, a, b, ALU.not_equal))
                            ch.after(nc.vector.tensor_scalar(flag, flag, NEG, None, ALU.mult))
                        for g in range(GROUPS):
                            v.wait_ge(turned, g + 1)
                            for k, table in enumerate((src_idx, dst_rel, dist_w)):
                                last = nc.vector.tensor_copy(table[:].rearrange("p (q g) -> p g q", g=GROUPS)[:, g, :], ps_t[:, g % 2, k, :])
                            last.then_inc(taken, 1)
                        dve_total[0] = ch.n

                    @block.tensor
                    def _(pe):
                        pe.wait_ge(key_ready, 1)
                        nc.tensor.matmul(ps[:, 8:9], prev_m[:], key[:, SLOTS:SLOTS + 1], start=True, stop=True)
                        nc.tensor.matmul(ps[:, 9:10], next_m[:], key[:, 1:2], start=True, stop=True).then_inc(moved, 1)
                        for g in range(GROUPS):
                            if g >= 2:
                                pe.wait_ge(taken, g - 1)
                            for k, field in enumerate((rows[:, g, 0, :], rel_row[:, g, :], rows[:, g, 3, :])):
                                last = nc.tensor.transpose(ps_t[:, g % 2, k, :], field, ident[:])
                            last.then_inc(turned, 1)

        q_sb = node_acc[:].rearrange("p j n -> p (j n)")[:, 0:NODE_TILES * D].rearrange("p (j n) -> p j n", n=D)
        rel4 = tile(top, "rel4", [P, HEADS, HD])
        with ExitStack() as ctx:
            w_sb = carve(scores_flat, [P, FC, 3 * D], start=0)
            bias_sb = carve(scores_flat, [P, 3 * D])
            xb = carve(scores_flat, [P, 2, BATCH, D])
            xt = carve(scores_flat, [P, 2, FC * P])
            kv = [carve(ring_flat, [P, 2, BATCH, D], start=0), tile(ctx, "kv", [P, 2, BATCH, D])[:]]
            b_row = tile(ctx, "b_row", [1, 3 * D])
            q_col = tile(ctx, "q_col", [P, FC])
            q_all = tile(ctx, "q_all", [P, FC, P])
            rel_sb = tile(ctx, "rel_sb", [P, HD])
            ps_x = bank(ctx, "ps_x", [P, 2, 512])
            ps_qkv = bank(ctx, "ps_qkv", [P, 2, 1024])
            w_landed, w_ready, bias_ready, x_pad = sem("w_landed"), sem("w_ready"), sem("bias_ready"), sem("x_pad")
            x_landed = [sem("x_landed0"), sem("x_landed1")]
            kv_stored = [sem("kv_stored0"), sem("kv_stored1")]
            x_turned, xt_ready, qkv_done, qkv_taken = sem("x_turned"), sem("xt_ready"), sem("qkv_done"), sem("qkv_taken")

            def rows_of(dram, tile0, n):
                return dram[bass.DynSlice(tile0 * P, n * P), :].rearrange("(t p) d -> p t d", p=P)

            with nc.Block() as block:

                @block.sync
                def _(sp):
                    for k, w in enumerate((wq, wk, wv)):
                        sp.dma_start(w_sb[:, :, k * D:(k + 1) * D], w.rearrange("(c p) n -> p c n", p=P)).then_inc(w_landed, 16)
                    for k, b in enumerate((bq, bk, bv)):
                        sp.dma_start(b_row[0:1, k * D:(k + 1) * D], row(b)).then_inc(w_landed, 16)
                    for c in range(FC):
                        sp.dma_start(q_col[:, c:c + 1], query[c * P:(c + 1) * P].rearrange("(p a) -> p a", a=1)).then_inc(w_landed, 16)
                    sp.dma_start(rel_sb[0:REL, :], rel_w).then_inc(w_landed, 16)

                    def load(it, h, last=False):
                        b = it * 2 + h
                        full = BATCH - 1 if last else BATCH
                        sp.dma_start(xb[:, h, 0:full, :], rows_of(x, b * BATCH, full)).then_inc(x_landed[h], 16)
                        if last:
                            sp.wait_ge(x_pad, 1)
                            sp.dma_start(xb[0:LAST_ROWS, h, full, :], x[(NODE_TILES - 1) * P:N, :]).then_inc(x_landed[h], 16)

                    def store(it, h):
                        b = it * 2 + h
                        sp.wait_ge(qkv_taken, (b + 1) * BATCH)
                        for k, dram in enumerate((k_d, v_d)):
                            sp.dma_start(rows_of(dram, b * BATCH, BATCH), kv[h][:, k]).then_inc(kv_stored[h], 16)

                    load(0, 0)
                    load(0, 1)
                    with sp.Fori(0, PAIRS - 2) as it:
                        for h in range(2):
                            store(it, h)
                            load(it + 1, h)
                    store(PAIRS - 2, 0)
                    load(PAIRS - 1, 0)
                    store(PAIRS - 2, 1)
                    load(PAIRS - 1, 1, last=True)
                    for h in range(2):
                        store(PAIRS - 1, h)
                    for h in range(2):
                        sp.wait_ge(kv_stored[h], 32 * PAIRS)

                @block.vector
                def _(v):
                    ch = chain(v, c_dve, dve_total)
                    ch.after(nc.vector.memset(rel4[:], 0.0))
                    v.wait_ge(w_landed, 9 * 16)
                    for c in range(FC):
                        ch.after(nc.vector.tensor_scalar(q_all[:, c, :], ident[:], 0.0, q_col[:, c:c + 1], ALU.mult, ALU.add))
                        ch.after(nc.vector.tensor_scalar(q_all[:, c, :], q_all[:, c, :], 0.1, None, ALU.mult))
                    for h in range(HEADS):
                        nc.vector.tensor_scalar(rel4[0:REL, h, :], rel_sb[0:REL, :], 0.2, None, ALU.mult)
                    v.sem_inc(w_ready, 1)
                    v.wait_ge(bias_ready, 1)
                    ch.after(nc.vector.tensor_copy(bias_sb[:], ps_qkv[:, 0, 0:3 * D]))
                    v.sem_inc(bias_ready, 1)

                    def take(it, h, first=False):
                        b = it * 2 + h
                        if not first:
                            v.wait_ge(kv_stored[h], 32 * it)
                        for t in range(BATCH):
                            n = b * BATCH + t
                            s = (h * BATCH + t) % 2
                            v.wait_ge(qkv_done, n + 1)
                            nc.vector.tensor_tensor(q_sb[:, bass.DynSlice(n, 1), :], ps_qkv[:, s, 0:D].unsqueeze(1),
                                                    bias_sb[:, 0:D].unsqueeze(1), ALU.add)
                            nc.vector.tensor_tensor(kv[h][:, :, t, :], ps_qkv[:, s, D:3 * D].rearrange("p (k d) -> p k d", d=D),
                                                    bias_sb[:, D:3 * D].rearrange("p (k d) -> p k d", d=D), ALU.add).then_inc(qkv_taken, 1)

                    take(0, 0, first=True)
                    take(0, 1, first=True)
                    with v.Fori(1, PAIRS - 1) as it:
                        take(it, 0)
                        take(it, 1)
                    v.wait_ge(x_turned, (2 * PAIRS - 2) * BATCH)
                    nc.vector.memset(xb[:, 1, BATCH - 1, :], 0.0).then_inc(x_pad, 1)
                    take(PAIRS - 1, 0)
                    take(PAIRS - 1, 1)
                    dve_total[0] = ch.n

                @block.scalar
                def _(act):
                    def evacuate(it):
                        for t in range(2 * BATCH):
                            n = it * 2 * BATCH + t
                            act.wait_ge(x_turned, n + 1)
                            nc.scalar.activation(xt[:, t % 2, :], ps_x[:, t % 2, 0:FC * P], ACT.Copy).then_inc(xt_ready, 1)

                    with act.Fori(0, PAIRS) as it:
                        evacuate(it)

                @block.tensor
                def _(pe):
                    pe.wait_ge(w_ready, 1)
                    for lo, hi in ((0, 512), (512, 3 * D)):
                        for c in range(FC):
                            nc.tensor.matmul(ps_qkv[:, 0, lo:hi], q_all[:, c, :], w_sb[:, c, lo:hi], start=c == 0, stop=False)
                        last = nc.tensor.matmul(ps_qkv[:, 0, lo:hi], ones_row[0:1, :], b_row[0:1, lo:hi], start=False, stop=True)
                    last.then_inc(bias_ready, 1)
                    pe.wait_ge(bias_ready, 2)

                    def turn(n, h, t, slot, prior):
                        if prior:
                            pe.wait_ge(xt_ready, n - 1)
                        for c in range(FC):
                            last = nc.tensor.transpose(ps_x[:, slot, c * P:(c + 1) * P], xb[:, h, t, c * P:(c + 1) * P], ident[:])
                        last.then_inc(x_turned, 1)

                    def project(it, first=False, last=False):
                        for k in range(2 * BATCH):
                            n = it * 2 * BATCH + k
                            h, t = divmod((k + 1) % (2 * BATCH), BATCH)
                            if not (last and k == 2 * BATCH - 1):
                                if t == 0:
                                    pe.wait_ge(x_landed[h], (it if h else it + 1) * 16 + (32 if last and h else 16))
                                turn(n + 1, h, t, (k + 1) % 2, not (first and k == 0))
                            pe.wait_ge(xt_ready, n + 1)
                            if not (first and k < 2):
                                pe.wait_ge(qkv_taken, n - 1)
                            for lo, hi in ((0, 512), (512, 3 * D)):
                                for c in range(FC):
                                    mm = nc.tensor.matmul(ps_qkv[:, k % 2, lo:hi], xt[:, k % 2, c * P:(c + 1) * P], w_sb[:, c, lo:hi],
                                                          start=c == 0, stop=c == FC - 1)
                            mm.then_inc(qkv_done, 1)

                    pe.wait_ge(x_landed[0], 16)
                    turn(0, 0, 0, 0, False)
                    project(0, first=True)
                    with pe.Fori(1, PAIRS - 1) as it:
                        project(it)
                    project(PAIRS - 1, last=True)

        def load_indices(sp, it, h, base, first):
            if not first:
                for u in range(h * HALF, (h + 1) * HALF):
                    sp.wait_ge(gathered[u], base + it * 16)
            sp.dma_start(idx_now[:, h, :], src_idx[:, bass.DynSlice(it * BODY + h * HALF, HALF)]).then_inc(idx_landed[h], 16)

        def gather_rows(dram, h, u):
            nc.gpsimd.indirect_dma_start(out=ring[:, u, 0:D], out_offset=None, in_=dram, in_offset=bass.IndirectOffsetOnAxis(
                ap=idx_now[:, h, u % HALF:u % HALF + 1], axis=0)).then_inc(gathered[u], 16)

        def gather_first(pool, dram, base):
            for h in range(2):
                pool.wait_ge(idx_landed[h], base + 16)
                pool.sem_inc(half_begun, 1)
                for u in range(h * HALF, (h + 1) * HALF):
                    gather_rows(dram, h, u)

        def load_nodes(engine, step, n):
            return nc.values_load_multi_w_load_instructions(
                step_node[0:1, bass.DynSlice(step, n)], engines=[engine], min_val=0, max_val=NODE_TILES - 1,
                skip_runtime_bounds_check_because="the table is clamped to the node tiles")[1]

        with ExitStack() as ctx:
            match_b = tile(ctx, "match_b", [P, 2, HALF, 2 * P], BF16)
            diff = tile(ctx, "diff", [P, 4, 2 * P], BF16)
            onehot = tile(ctx, "onehot", [P, 2, 4, 2 * P])
            prod = tile(ctx, "prod", [P, 3, 2 * D])
            ps_q = bank(ctx, "ps_q", [P, 4, 2 * D])
            ps_r = bank(ctx, "ps_r", [P, 4, 2 * D])
            match_landed = [sem("match_landed0"), sem("match_landed1")]
            diff_ready, onehot_ready, pair_ready = sem("diff_ready"), sem("onehot_ready"), sem("pair_ready")
            keys_ready, prods_ready, pairs_scored = sem("keys_ready"), sem("prods_ready"), sem("pairs_scored")
            match_rows = match_d.rearrange("s n -> (s n)")

            with nc.Block() as block:

                @block.sync
                def _(sp):
                    def tables(it, first=False):
                        for h in range(2):
                            if not first:
                                sp.wait_ge(onehot_ready, it * 4 + 2 * h - 2)
                            sp.dma_start(match_b[:, h].rearrange("p s n -> p (s n)"),
                                         match_rows[bass.DynSlice((it * BODY + h * HALF) * 2 * P, HALF * 2 * P)].partition_broadcast(P)
                                         ).then_inc(match_landed[h], 16)
                            load_indices(sp, it, h, 0, first)

                    tables(0, first=True)
                    with sp.Fori(1, ITERS) as it:
                        tables(it)

                @block.gpsimd
                def _(pool):
                    def gather(it, first=False):
                        for h in range(2):
                            pool.wait_ge(idx_landed[h], it * 16 + 16)
                            if not first:
                                pool.wait_ge(keys_ready, it * 8 - 4 + 4 * h)
                            pool.sem_inc(half_begun, 1)
                            for u in range(h * HALF, (h + 1) * HALF):
                                gather_rows(k_d, h, u)

                    gather(0, first=True)
                    with pool.Fori(1, ITERS) as it:
                        gather(it)

                @block.scalar
                def _(act):
                    def match(it, first=False):
                        for g in range(4):
                            h = g // 2
                            if g % 2 == 0:
                                act.wait_ge(match_landed[h], it * 16 + 16)
                            if not (first and g == 0):
                                act.wait_ge(onehot_ready, it * 4 + g)
                            nc.scalar.activation(diff[:], match_b[:, h, (g % 2) * 4:(g % 2) * 4 + 4, :], ACT.Abs,
                                                 bias=neg_row_id[:, 0:1]).then_inc(diff_ready, 1)
                            act.wait_ge(diff_ready, it * 4 + g + 1)
                            if not (first and g < 2):
                                act.wait_ge(pair_ready, it * 8 + 2 * g - 2)
                            nc.scalar.activation(onehot[:, g % 2], diff[:], ACT.Relu, bias=1.0, scale=-1.0).then_inc(onehot_ready, 1)

                    match(0, first=True)
                    with act.Fori(1, ITERS) as it:
                        match(it)

                @block.tensor
                def _(pe):
                    def spread(it, first=False):
                        for u in range(BODY):
                            g, pr, k = u // 4, u // 2, u % 4
                            if u % HALF == 0:
                                nodes = load_nodes(ENGINE.PE, it * BODY + u, HALF)
                            if k == 0:
                                pe.wait_ge(onehot_ready, it * 4 + g + 1)
                            if u % 2 == 0 and not (first and pr < 4):
                                pe.wait_ge(prods_ready, it * 8 + pr - 3)
                            at = (u % 2) * D
                            nc.tensor.matmul(ps_q[:, pr % 4, at:at + D], onehot[:, g % 2, k, 0:P],
                                             q_sb[:, bass.DynSlice(nodes[u % HALF], 1), :].rearrange("p a n -> p (a n)"),
                                             start=True, stop=True)
                            last = nc.tensor.matmul(ps_r[:, pr % 4, at:at + D], onehot[:, g % 2, k, P:2 * P],
                                                    rel4[:].rearrange("p h d -> p (h d)"), start=True, stop=True)
                            if u % 2:
                                last.then_inc(pair_ready, 1)

                    spread(0, first=True)
                    with pe.Fori(1, ITERS) as it:
                        spread(it)

                @block.vector
                def _(v):
                    def score(it, first=False):
                        def keys(pr):
                            for u in (2 * pr, 2 * pr + 1):
                                v.wait_ge(gathered[u], it * 16 + 16)
                            v.wait_ge(pair_ready, it * 8 + pr + 1)
                            if not (first and pr < 3):
                                v.wait_ge(pairs_scored, it * 8 + pr - 2 if pr >= 3 else it * 8)
                            nc.vector.tensor_tensor(prod[:, pr % 3].rearrange("p (a n) -> p a n", n=D), ring[:, 2 * pr:2 * pr + 2, 0:D],
                                                    ps_r[:, pr % 4].rearrange("p (a n) -> p a n", n=D), ALU.add).then_inc(keys_ready, 1)

                        def products(pr):
                            v.wait_ge(keys_ready, it * 8 + pr + 1)
                            nc.vector.tensor_tensor(prod[:, pr % 3], prod[:, pr % 3], ps_q[:, pr % 4], ALU.mult).then_inc(prods_ready, 1)

                        def sums(pr):
                            v.wait_ge(prods_ready, it * 8 + pr + 1)
                            nc.vector.tensor_reduce(scores[:, bass.DynSlice(it * BODY + 2 * pr, 2), :],
                                                    prod[:, pr % 3].rearrange("p (a h d) -> p a h d", a=2, h=HEADS),
                                                    AX.X, ALU.add).then_inc(pairs_scored, 1)

                        for pr in range(10):
                            if pr < 8:
                                keys(pr)
                            if 1 <= pr < 9:
                                products(pr - 1)
                            if pr >= 2:
                                sums(pr - 2)

                    score(0, first=True)
                    with v.Fori(1, ITERS) as it:
                        score(it)

        with ExitStack() as ctx:
            srow = carve(acc_flat, [P, HEADS, SLOTS], start=0)
            fw = carve(acc_flat, [P, HEADS, SLOTS])
            top_s = carve(acc_flat, [P, HEADS, SLOTS])
            init_fw = tile(ctx, "init_fw", [P, HEADS])
            init_bw = tile(ctx, "init_bw", [P, HEADS])
            carry4 = tile(ctx, "carry4", [P, 2, HEADS])
            ends = tile(ctx, "ends", [HEADS, 4, P])
            chain4 = tile(ctx, "chain4", [HEADS, 2, P + 1])
            ps_s = bank(ctx, "ps_s", [P, 4, 512])
            ps_e = bank(ctx, "ps_e", [P, 512])
            ps_i = bank(ctx, "ps_i", [P, 512])
            rows_turned, rows_taken, ends_ready, ends_turned, chain_ready, init_turned = (
                sem("rows_turned"), sem("rows_taken"), sem("ends_ready"), sem("ends_turned"), sem("chain_ready"), sem("init_turned"))
            shifted, exp_ready, back_turned, back_taken = sem("shifted"), sem("exp_ready"), sem("back_turned"), sem("back_taken")
            by_group = scores[:].rearrange("p (q g) h -> p g h q", g=GROUPS)
            units = [(h, g0, min(4, GROUPS - g0)) for h in range(HEADS) for g0 in range(0, GROUPS, 4)]
            per_head = len(units) // HEADS

            with nc.Block() as block:

                @block.sync
                def _(sp):
                    for h in range(2):
                        load_indices(sp, 0, h, ITERS * 16, True)

                @block.gpsimd
                def _(pool):
                    gather_first(pool, v_d, ITERS * 16)

                @block.tensor
                def _(pe):
                    for i, (h, g0, n) in enumerate(units):
                        if i >= 4:
                            pe.wait_ge(rows_taken, i - 3)
                        for k in range(n):
                            last = nc.tensor.transpose(ps_s[:, i % 4, k * P:(k + 1) * P], by_group[:, g0 + k, h, :], ident[:])
                        last.then_inc(rows_turned, 1)
                    for way in range(2):
                        src_end = fw[:, :, SLOTS - 1] if way == 0 else top_s[:, :, 0]
                        pe.wait_ge(ends_ready, way + 1)
                        nc.tensor.transpose(ps_e[0:HEADS, 2 * way * P:(2 * way + 1) * P], src_end, ident[:])
                        nc.tensor.transpose(ps_e[0:HEADS, (2 * way + 1) * P:(2 * way + 2) * P], carry4[:, way, :], ident[:]).then_inc(ends_turned, 1)
                        pe.wait_ge(chain_ready, way + 1)
                        nc.tensor.transpose(ps_i[:, way * HEADS:(way + 1) * HEADS], chain4[:, way, way:way + P],
                                            ident[0:HEADS, 0:HEADS]).then_inc(init_turned, 1)
                    for i, (h, g0, n) in enumerate(units):
                        pe.wait_ge(exp_ready, h + 1)
                        if i >= 4:
                            pe.wait_ge(back_taken, i - 3)
                        for k in range(n):
                            last = nc.tensor.transpose(ps_s[:, i % 4, k * P:(k + 1) * P], srow[:, h, (g0 + k) * P:(g0 + k + 1) * P], ident[:])
                        last.then_inc(back_turned, 1)

                @block.scalar
                def _(act):
                    for i, (h, g0, n) in enumerate(units):
                        act.wait_ge(rows_turned, i + 1)
                        nc.scalar.activation(srow[:, h, g0 * P:(g0 + n) * P], ps_s[:, i % 4, 0:n * P], ACT.Copy).then_inc(rows_taken, 1)
                    for h in range(HEADS):
                        act.wait_ge(shifted, h + 1)
                        nc.scalar.activation(srow[:, h], srow[:, h], ACT.Exp, scale=SCALE).then_inc(exp_ready, 1)

                @block.vector
                def _(v):
                    ch = chain(v, c_dve, dve_total)
                    nc.vector.tensor_scalar(carry4[:, 0, :], ident[:, 0:HEADS], 0.0, carry_fw[:, 0:1], ALU.mult, ALU.add)
                    nc.vector.tensor_scalar(carry4[:, 1, :], ident[:, 0:HEADS], 0.0, carry_bw[:, 0:1], ALU.mult, ALU.add)
                    ch.after(nc.vector.memset(chain4[:], NEG))
                    for h in range(HEADS):
                        v.wait_ge(rows_taken, per_head * (h + 1))
                        ch.after(nc.vector.tensor_tensor_scan(fw[:, h], same_prev, srow[:, h], NEG, ALU.add, ALU.max))
                    v.sem_inc(ends_ready, 1)

                    def carry(way):
                        v.wait_ge(ends_turned, way + 1)
                        ch.after(nc.vector.tensor_copy(ends[:, 2 * way:2 * way + 2, :].rearrange("p a n -> p (a n)"),
                                                       ps_e[0:HEADS, 2 * way * P:(2 * way + 2) * P]))
                        order = slice(None, None, -1) if way else slice(None)
                        run = chain4[:, way, 0:P] if way else chain4[:, way, 1:P + 1]
                        ch.after(nc.vector.tensor_tensor_scan(run[:, order], ends[:, 2 * way + 1][:, order],
                                                              ends[:, 2 * way][:, order], NEG, ALU.add, ALU.max))
                        v.sem_inc(chain_ready, 1)
                        v.wait_ge(init_turned, way + 1)
                        ch.after(nc.vector.tensor_copy((init_bw if way else init_fw)[:], ps_i[:, way * HEADS:(way + 1) * HEADS]))

                    carry(0)
                    for h in range(HEADS):
                        ch.after(nc.vector.tensor_tensor_scan(fw[:, h], same_prev, srow[:, h], init_fw[:, h:h + 1], ALU.add, ALU.max))
                    back = slice(None, None, -1)
                    for h in range(HEADS):
                        ch.after(nc.vector.tensor_tensor_scan(top_s[:, h][:, back], same_next[:, ::-1], fw[:, h][:, back], NEG, ALU.add, ALU.max))
                    v.sem_inc(ends_ready, 1)
                    carry(1)
                    for h in range(HEADS):
                        ch.after(nc.vector.tensor_tensor_scan(top_s[:, h][:, back], same_next[:, ::-1], fw[:, h][:, back],
                                                              init_bw[:, h:h + 1], ALU.add, ALU.max))
                        nc.vector.tensor_tensor(srow[:, h], srow[:, h], top_s[:, h], ALU.subtract).then_inc(shifted, 1)
                    for i, (h, g0, n) in enumerate(units):
                        v.wait_ge(back_turned, i + 1)
                        nc.vector.tensor_copy(by_group[:, g0:g0 + n, h, :], ps_s[:, i % 4, 0:n * P].rearrange("p (g q) -> p g q", q=P)).then_inc(back_taken, 1)
                    dve_total[0] = ch.n

        def summing(layer):
            base = (layer + 1) * ITERS * 16
            rows_d, wide = (v_d, ACCW) if layer == 0 else (x1_d, D + 1)
            with ExitStack() as ctx:
                onehot = tile(ctx, f"onehot_{layer}", [P, 8, P])
                weighed = tile(ctx, f"weighed_{layer}", [P, 8, ACCW]) if layer == 0 else None
                apart = tile(ctx, f"apart_{layer}", [P, 4, P]) if layer == 0 else None
                apart_ready = sem(f"apart_ready_{layer}")
                ps_sum = bank(ctx, f"ps_sum_{layer}", [P, 8, 512])
                cleared, ones_set, onehot_ready, weighed_ready, w_copied, summed, added = (
                    sem(f"cleared_{layer}"), sem(f"ones_set_{layer}"), sem(f"onehot_ready_{layer}"), sem(f"weighed_ready_{layer}"),
                    sem(f"w_copied_{layer}"), sem(f"summed_{layer}"), sem(f"added_{layer}"))

                dve_part = NODE_TILES * ACCW // 2

                with nc.Block() as block:

                    @block.sync
                    def _(sp):
                        def tables(it, first=False):
                            for h in range(2):
                                load_indices(sp, it, h, base, first)

                        if layer == 1:
                            tables(0, first=True)
                        with sp.Fori(1, ITERS) as it:
                            tables(it)

                    @block.gpsimd
                    def _(pool):
                        def gather(it):
                            for h in range(2):
                                pool.wait_ge(idx_landed[h], base + it * 16 + 16)
                                if layer == 0:
                                    pool.wait_ge(weighed_ready, it * 4 - 2 + 2 * h)
                                else:
                                    pool.wait_ge(summed, it * BODY - HALF + HALF * h)
                                pool.sem_inc(half_begun, 1)
                                for u in range(h * HALF, (h + 1) * HALF):
                                    gather_rows(rows_d, h, u)

                        if layer == 1:
                            gather_first(pool, rows_d, base)
                        with pool.Fori(1, ITERS) as it:
                            gather(it)

                    @block.scalar
                    def _(act):
                        nc.scalar.activation(acc_flat[:, dve_part:], zero_col[:].to_broadcast([P, NODE_TILES * ACCW - dve_part]),
                                             ACT.Copy).then_inc(cleared, 1)

                        def match(it, first=False):
                            for g in range(4):
                                for k in range(4):
                                    if k == 0 and not (first and g == 0):
                                        act.wait_ge(onehot_ready, it * 4 + g)
                                    s = it * BODY + 4 * g + k
                                    last = nc.scalar.activation(apart[:, k], col_id[:], ACT.Abs, bias=dst_rel[:, bass.DynSlice(s, 1)], scale=-1.0)
                                last.then_inc(apart_ready, 1)
                                act.wait_ge(apart_ready, it * 4 + g + 1)
                                if not (first and g < 2):
                                    act.wait_ge(summed, it * BODY + 4 * g - 4)
                                half = (g % 2) * 4
                                nc.scalar.activation(onehot[:, half:half + 4], apart[:], ACT.Relu, bias=1.0, scale=-1.0).then_inc(onehot_ready, 1)

                        if layer == 0:
                            match(0, first=True)
                            with act.Fori(1, ITERS) as it:
                                match(it)

                    @block.vector
                    def _(v):
                        nc.vector.memset(ring[:, :, D:D + 1], 1.0).then_inc(ones_set, 1)
                        nc.vector.memset(acc_flat[:, 0:dve_part], 0.0).then_inc(cleared, 1)
                        v.wait_ge(cleared, 2)

                        def match(it, g):
                            if layer == 1:
                                for u in range(4 * g, 4 * g + 4):
                                    s = it * BODY + u
                                    nc.vector.tensor_scalar(onehot[:, u % 8], col_id[:], dst_rel[:, bass.DynSlice(s, 1)],
                                                            dist_w[:, bass.DynSlice(s, 1)], ALU.is_equal, ALU.mult).then_inc(onehot_ready, 1)
                            else:
                                w = scores[:, bass.DynSlice(it * BODY + 4 * g, 4), :]
                                half = (g % 2) * 4
                                for u in range(4 * g, 4 * g + 4):
                                    v.wait_ge(gathered[u], base + it * 16 + 16)
                                nc.vector.tensor_copy(weighed[:, half:half + 4, D:ACCW], w).then_inc(w_copied, 1)
                                nc.vector.tensor_tensor(
                                    weighed[:, half:half + 4, 0:D].rearrange("p s (h d) -> p s h d", d=HD),
                                    ring[:, 4 * g:4 * g + 4, 0:D].rearrange("p s (h d) -> p s h d", d=HD),
                                    w.unsqueeze(3).to_broadcast([P, 4, HEADS, HD]), ALU.mult).then_inc(weighed_ready, 1)

                        def add(n, u, node, first=False):
                            v.wait_ge(summed, n + 1)
                            if not first:
                                v.wait_ge(added, n)
                            part = node_acc[:, bass.DynSlice(node, 1), 0:wide]
                            nc.vector.tensor_tensor(part, part, ps_sum[:, u % 8, 0:wide].unsqueeze(1), ALU.add).then_inc(added, 1)

                        match(0, 0)
                        for g in range(1, 4):
                            match(0, g)
                            nodes = load_nodes(ENGINE.DVE, 4 * (g - 1), 4)
                            for k in range(4):
                                u = 4 * (g - 1) + k
                                add(u, u, nodes[k], first=u == 0)
                        with v.Fori(1, ITERS) as it:
                            for g in range(4):
                                match(it, g)
                                if g % 2 == 0:
                                    nodes = load_nodes(ENGINE.DVE, it * BODY + 4 * g - 4, 8)
                                for k in range(4):
                                    u = 4 * (g - 1) + k
                                    add(it * BODY + u, u % BODY, nodes[(g % 2) * 4 + k])
                        nodes = load_nodes(ENGINE.DVE, STEPS - 4, 4)
                        for k in range(4):
                            add(STEPS - 4 + k, BODY - 4 + k, nodes[k])

                    @block.tensor
                    def _(pe):
                        if layer == 1:
                            pe.wait_ge(ones_set, 1)

                        def sums(it, first=False):
                            for u in range(BODY):
                                n = it * BODY + u
                                if layer == 1:
                                    pe.wait_ge(onehot_ready, n + 1)
                                elif u % 4 == 0:
                                    pe.wait_ge(onehot_ready, it * 4 + u // 4 + 1)
                                if layer == 0 and u % 4 == 0:
                                    pe.wait_ge(w_copied, it * 4 + u // 4 + 1)
                                    pe.wait_ge(weighed_ready, it * 4 + u // 4 + 1)
                                if layer == 1:
                                    pe.wait_ge(gathered[u], base + it * 16 + 16)
                                if not (first and u < 8):
                                    pe.wait_ge(added, n - 7)
                                edge_rows = weighed[:, u % 8, :] if layer == 0 else ring[:, u, :]
                                nc.tensor.matmul(ps_sum[:, u % 8, 0:wide], onehot[:, u % 8], edge_rows, start=True, stop=True).then_inc(summed, 1)

                        sums(0, first=True)
                        with pe.Fori(1, ITERS) as it:
                            sums(it)

        def node_stage(layer):
            tag = f"_n{layer}"
            in_d, out_d = (x, x1_d) if layer == 0 else (x1_d, out)
            gamma, beta = (gamma0, beta0) if layer == 0 else (gamma1, beta1)
            n_weights = 4 if layer == 0 else 7
            with ExitStack() as ctx:
                cols = BATCH * D
                res = carve(scores_flat, [P, 2, BATCH, D], start=0)
                msg = carve(scores_flat, [P, BATCH, D])
                xin = carve(ring_flat, [P, 2, BATCH, D], start=0)
                done = tile(ctx, "done" + tag, [P, BATCH, D])
                v_rows = tile(ctx, "v_rows" + tag, [P, BATCH, D]) if layer == 0 else None
                hid_t = tile(ctx, "hid_t" + tag, [P, FC, BATCH * P]) if layer else None
                msg_t = carve(flags_flat, [P, FC, BATCH * P], start=0)
                inv = carve(flags_flat, [P, NODE_TILES, HEADS])
                lone = carve(flags_flat, [P, NODE_TILES, HEADS])
                wa = carve(dst_rel[:], [P, FC, D], start=0) if layer else tile(ctx, "wa" + tag, [P, FC, D])
                wb = carve(dst_rel[:], [P, FC, D]) if layer else None
                raw = carve(dist_w[:], [P, 2, FC, D], start=0) if layer else None
                gamma_b = tile(ctx, "gamma_b" + tag, [P, D])
                beta_b = tile(ctx, "beta_b" + tag, [P, D])
                bias_row = tile(ctx, "bias_row" + tag, [1, D])
                b1_col = tile(ctx, "b1_col" + tag, [P, FC])
                stat = tile(ctx, "stat" + tag, [P, 2, BATCH, 6])
                mom = tile(ctx, "mom" + tag, [P, 2, BATCH, 2])
                scale_c = tile(ctx, "scale_c" + tag, [P, 2, BATCH, 4])
                ps_x = bank(ctx, "ps_x" + tag, [P, 2, 512])
                ps_h = bank(ctx, "ps_h" + tag, [P, 2, 512])
                ps_o = bank(ctx, "ps_o" + tag, [P, 4, 512])
                S = {k: sem(k + tag) for k in (
                    "w_landed", "w_turned", "w_ready", "stored", "x_landed0", "x_landed1", "v_landed", "v_masked", "padded",
                    "inv_ready", "summed", "msg_ready", "msg_turned", "msg_t_ready", "hid_done", "hid_ready", "out_done",
                    "res_ready", "beta_added", "stats", "moments", "stats_seen", "var1", "var2", "std1", "std2", "inv_std",
                    "scale1", "scale2", "normed1", "normed2", "scaled", "second_in", "prep")}

                def batch_rows(dram, b, full=BATCH):
                    return dram[bass.DynSlice(b * (BATCH * P), full * P), :].rearrange("(t p) d -> p t d", p=P)

                with nc.Block() as block:

                    @block.sync
                    def _(sp):
                        def load_x(b, par, last=False):
                            full = BATCH
                            if last and layer == 0:
                                full = BATCH - 1
                                sp.wait_ge(S["padded"], 1)
                                sp.dma_start(xin[0:LAST_ROWS, par, full, :], in_d[(NODE_TILES - 1) * P:N, :]).then_inc(S[f"x_landed{par}"], 16)
                            sp.dma_start(xin[:, par, 0:full], batch_rows(in_d, b, full)).then_inc(S[f"x_landed{par}"], 16)

                        def load_v(b):
                            sp.dma_start(v_rows[:], batch_rows(v_d, b)).then_inc(S["v_landed"], 16)

                        def store(b, last=False):
                            sp.wait_ge(S["normed2"], (b + 1) * BATCH)
                            full = BATCH - 1 if last and layer == 1 else BATCH
                            sp.dma_start(batch_rows(out_d, b, full), done[:, 0:full]).then_inc(S["stored"], 16)
                            if last and layer == 1:
                                sp.dma_start(out_d[(NODE_TILES - 1) * P:N, :], done[0:LAST_ROWS, full, :]).then_inc(S["stored"], 16)

                        def turn(k, par, v=True, x=True, last_x=False):
                            if v and layer == 0:
                                sp.wait_ge(S["msg_ready"], k + 2)
                                load_v(k + 2)
                            if x:
                                sp.wait_ge(S["second_in"], k)
                                load_x(k + 1, 1 - par, last_x)
                            store(k - 1)

                        if layer == 0:
                            load_v(0)
                            sp.dma_start(wa[:], wo.rearrange("(c p) n -> p c n", p=P)).then_inc(S["w_landed"], 16)
                        else:
                            sp.dma_start(raw[:, 0], w1.rearrange("(c p) n -> p c n", p=P)).then_inc(S["w_landed"], 16)
                            sp.dma_start(raw[:, 1], w2.rearrange("(c p) n -> p c n", p=P)).then_inc(S["w_landed"], 16)
                            for c in range(FC):
                                sp.dma_start(b1_col[:, c:c + 1], b1[c * P:(c + 1) * P].rearrange("(p a) -> p a", a=1)).then_inc(S["w_landed"], 16)
                        sp.dma_start(bias_row[:], row(b2 if layer else bo)).then_inc(S["w_landed"], 16)
                        sp.dma_start(gamma_b[:], gamma.partition_broadcast(P)).then_inc(S["w_landed"], 16)
                        sp.dma_start(beta_b[:], beta.partition_broadcast(P)).then_inc(S["w_landed"], 16)
                        load_x(0, 0)
                        load_x(1, 1)
                        if layer == 0:
                            sp.wait_ge(S["msg_ready"], 1)
                            load_v(1)
                            sp.wait_ge(S["msg_ready"], 2)
                            load_v(2)
                        with sp.Fori(0, PAIRS - 2) as i:
                            turn(2 * i + 1, 1)
                            turn(2 * i + 2, 0)
                        turn(BATCHES - 3, 1)
                        turn(BATCHES - 2, 0, v=False, last_x=True)
                        turn(BATCHES - 1, 1, v=False, x=False)
                        store(BATCHES - 1, last=True)
                        sp.wait_ge(S["stored"], 16 * BATCHES + 16 * layer)

                    @block.gpsimd
                    def _(pool):
                        pool.wait_ge(S["w_landed"], n_weights * 16)
                        if layer == 0:
                            pool.wait_ge(S["inv_ready"], 1)

                        def mask_v(b):
                            if layer == 0:
                                pool.wait_ge(S["v_landed"], b * 16 + 16)
                                by_head = v_rows[:].rearrange("p t (h d) -> p (t h) d", d=HD)
                                nc.gpsimd.tensor_tensor(
                                    by_head, by_head, lone[:, bass.DynSlice(b * BATCH, BATCH), :].rearrange("p t h -> p (t h)").unsqueeze(2).to_broadcast(
                                        [P, BATCH * HEADS, HD]), ALU.mult).then_inc(S["v_masked"], 1)

                        def add_beta(b, par):
                            pool.wait_ge(S["res_ready"], b * 4 + 4)
                            nc.gpsimd.tensor_tensor(xin[:, par], xin[:, par], beta_b[:].unsqueeze(1).to_broadcast([P, BATCH, D]),
                                                    ALU.add).then_inc(S["beta_added"], 1)

                        mask_v(0)
                        with pool.Fori(0, PAIRS - 1) as i:
                            mask_v(2 * i + 1)
                            add_beta(2 * i, 0)
                            mask_v(2 * i + 2)
                            add_beta(2 * i + 1, 1)
                        mask_v(BATCHES - 1)
                        add_beta(BATCHES - 2, 0)
                        add_beta(BATCHES - 1, 1)

                    @block.tensor
                    def _(pe):
                        pe.wait_ge(S["w_landed"], n_weights * 16)
                        if layer == 1:
                            for k in range(2):
                                for c in range(FC):
                                    for i in range(FC):
                                        last = nc.tensor.transpose(ps_h[:, k, (i * FC + c) * P:(i * FC + c + 1) * P], raw[:, k, c, i * P:(i + 1) * P], ident[:])
                            last.then_inc(S["w_turned"], 1)
                            pe.wait_ge(S["w_ready"], 2)

                        def batch(b, par, first=False):
                            pe.wait_ge(S["msg_ready"], b + 1)
                            for t in range(BATCH):
                                slot = (par * BATCH + t) % 2
                                if not (first and t < 2):
                                    pe.wait_ge(S["msg_t_ready"], b * BATCH + t - 1)
                                for c in range(FC):
                                    last = nc.tensor.transpose(ps_x[:, slot, c * P:(c + 1) * P], msg[:, t, c * P:(c + 1) * P], ident[:])
                                last.then_inc(S["msg_turned"], 1)
                            rows_t = msg_t
                            pe.wait_ge(S["msg_t_ready"], (b + 1) * BATCH)
                            if layer == 1:
                                k = 0
                                for lo, hi in ((0, 4 * P), (4 * P, BATCH * P)):
                                    for o in range(FC):
                                        if not (first and k < 2):
                                            pe.wait_ge(S["hid_ready"], b * 4 + k - 1)
                                        for c in range(FC):
                                            last = nc.tensor.matmul(ps_h[:, k % 2, 0:hi - lo], wa[:, c, o * P:(o + 1) * P], msg_t[:, c, lo:hi],
                                                                    start=c == 0, stop=c == FC - 1)
                                        last.then_inc(S["hid_done"], 1)
                                        k += 1
                                rows_t = hid_t
                                pe.wait_ge(S["hid_ready"], b * 4 + 4)
                            if not first:
                                pe.wait_ge(S["res_ready"], b * 4)
                            w = wb if layer else wa
                            for t in range(BATCH):
                                o = ps_o[:, t // 2, (t % 2) * D:(t % 2 + 1) * D]
                                nc.tensor.matmul(o, ones_row[0:1, :], bias_row[0:1, :], start=True, stop=False)
                                for c in range(FC):
                                    last = nc.tensor.matmul(o, rows_t[:, c, t * P:(t + 1) * P], w[:, c, :], start=False, stop=c == FC - 1)
                                last.then_inc(S["out_done"], 1)

                        batch(0, 0, first=True)
                        batch(1, 1)
                        with pe.Fori(1, PAIRS) as i:
                            batch(2 * i, 0)
                            batch(2 * i + 1, 1)

                    @block.scalar
                    def _(act):
                        if layer == 1:
                            act.wait_ge(S["w_landed"], n_weights * 16)
                            act.wait_ge(S["w_turned"], 1)
                            for k, w in enumerate((wa, wb)):
                                nc.scalar.activation(w[:].rearrange("p c n -> p (c n)"), ps_h[:, k, :], ACT.Copy).then_inc(S["w_ready"], 1)

                        def copy_turned(b, par, first=False):
                            for t in range(BATCH):
                                act.wait_ge(S["msg_turned"], b * BATCH + t + 1)
                                if t == 0 and not first:
                                    act.wait_ge(*((S["hid_done"], b * 4) if layer else (S["out_done"], b * BATCH)))
                                nc.scalar.activation(msg_t[:, :, t * P:(t + 1) * P], ps_x[:, (par * BATCH + t) % 2, 0:FC * P].rearrange("p (c n) -> p c n", n=P),
                                                     ACT.Copy).then_inc(S["msg_t_ready"], 1)

                        def hidden(b, first=False):
                            if layer == 1:
                                if not first:
                                    act.wait_ge(S["out_done"], b * BATCH)
                                k = 0
                                for lo, hi in ((0, 4 * P), (4 * P, BATCH * P)):
                                    for o in range(FC):
                                        act.wait_ge(S["hid_done"], b * 4 + k + 1)
                                        nc.scalar.activation(hid_t[:, o, lo:hi], ps_h[:, k % 2, 0:hi - lo], ACT.Gelu, bias=b1_col[:, o:o + 1]).then_inc(S["hid_ready"], 1)
                                        k += 1

                        def root(b, r):
                            act.wait_ge(S[f"var{r + 1}"], b + 1)
                            nc.scalar.activation(scale_c[:, r, :, 1], scale_c[:, r, :, 0], ACT.Sqrt).then_inc(S[f"std{r + 1}"], 1)

                        def norm(b, par, r, first=False):
                            act.wait_ge(S[f"scale{r + 1}"], b + 1)
                            if r and not first:
                                act.wait_ge(S["stored"], b * 16)
                            for t in range(BATCH):
                                nc.scalar.activation(done[:, t] if r else res[:, par, t], res[:, par, t], ACT.Identity,
                                                     bias=scale_c[:, r, t, 3:4], scale=scale_c[:, r, t, 2:3]).then_inc(S[f"normed{r + 1}"], 1)

                        def turn(k, par, following=True, second=True, first=False):
                            if following:
                                copy_turned(k + 1, 1 - par)
                            root(k, 0)
                            if following:
                                hidden(k + 1)
                            if second:
                                root(k - 1, 1)
                                norm(k - 1, 1 - par, 1, first)
                            norm(k, par, 0)

                        copy_turned(0, 0, first=True)
                        hidden(0, first=True)
                        turn(0, 0, second=False)
                        turn(1, 1, first=True)
                        with act.Fori(1, PAIRS - 1) as i:
                            turn(2 * i, 0)
                            turn(2 * i + 1, 1)
                        turn(BATCHES - 2, 0)
                        turn(BATCHES - 1, 1, following=False)
                        root(BATCHES - 1, 1)
                        norm(BATCHES - 1, 1, 1)

                    @block.vector
                    def _(v):
                        if layer == 0:
                            den = node_acc[:, :, D:ACCW]
                            nc.vector.tensor_scalar(lone, den, 0.0, None, ALU.is_le).then_inc(S["prep"], 1)
                            v.wait_ge(S["prep"], 1)
                            nc.vector.tensor_tensor(inv, den, lone, ALU.add).then_inc(S["prep"], 1)
                            v.wait_ge(S["prep"], 2)
                            nc.vector.reciprocal(inv, inv).then_inc(S["inv_ready"], 1)
                        else:
                            nc.vector.tensor_scalar(inv[:, :, 0], node_acc[:, :, D], 1e-6, None, ALU.max).then_inc(S["prep"], 1)
                            v.wait_ge(S["prep"], 1)
                            nc.vector.reciprocal(inv[:, :, 0], inv[:, :, 0]).then_inc(S["inv_ready"], 1)
                        v.wait_ge(S["inv_ready"], 1)
                        v.wait_ge(S["w_landed"], n_weights * 16)

                        def messages(b, first=False):
                            if not first:
                                v.wait_ge(S["msg_turned"], b * BATCH)
                            sums = node_acc[:, bass.DynSlice(b * BATCH, BATCH), 0:D]
                            if layer == 0:
                                nc.vector.tensor_tensor(
                                    msg[:].rearrange("p t (h d) -> p t h d", d=HD), sums.rearrange("p t (h d) -> p t h d", d=HD),
                                    inv[:, bass.DynSlice(b * BATCH, BATCH), :].unsqueeze(3).to_broadcast([P, BATCH, HEADS, HD]),
                                    ALU.mult).then_inc(S["summed"], 1)
                                v.wait_ge(S["summed"], b + 1)
                                v.wait_ge(S["v_masked"], b + 1)
                                nc.vector.tensor_tensor(msg[:], msg[:], v_rows[:], ALU.add).then_inc(S["msg_ready"], 1)
                            else:
                                nc.vector.tensor_tensor(msg[:], sums, inv[:, bass.DynSlice(b * BATCH, BATCH), 0:1].to_broadcast([P, BATCH, D]),
                                                        ALU.mult).then_inc(S["msg_ready"], 1)

                        def moments(b, par, r, n):
                            for t in range(BATCH):
                                op = nc.vector.bn_stats(stat[:, r, t], res[:, par, t])
                            op.then_inc(S["stats"], 1)
                            v.wait_ge(S["stats"], n + 1)
                            v.sem_inc(S["stats_seen"], 1)
                            for t in range(BATCH):
                                op = nc.vector.bn_aggr(mom[:, r, t], stat[:, r, t])
                            op.then_inc(S["moments"], 1)
                            v.wait_ge(S["moments"], n + 1)
                            nc.vector.tensor_scalar(scale_c[:, r, :, 0], mom[:, r, :, 1], EPS, None, ALU.add).then_inc(S[f"var{r + 1}"], 1)

                        def residual(b, par, n, last=False, early=False):
                            v.wait_ge(S[f"x_landed{par}"], (b - par) * 8 + (32 if last and layer == 0 else 16))
                            if not early:
                                v.wait_ge(S["normed2"], b * BATCH - BATCH)
                            for t in range(0, BATCH, 2):
                                m = min(2, BATCH - t)
                                v.wait_ge(S["out_done"], b * BATCH + t + m)
                                nc.vector.tensor_tensor(res[:, par, t:t + m], ps_o[:, t // 2, 0:m * D].rearrange("p (t d) -> p t d", d=D),
                                                        xin[:, par, t:t + m], ALU.add).then_inc(S["res_ready"], 1)
                            v.wait_ge(S["res_ready"], b * 4 + 4)
                            moments(b, par, 0, n)

                        def second(b, par, n):
                            v.wait_ge(S["normed1"], (b + 1) * BATCH)
                            nc.vector.tensor_tensor(res[:, par], res[:, par], gamma_b[:].unsqueeze(1).to_broadcast([P, BATCH, D]),
                                                    ALU.mult).then_inc(S["scaled"], 1)
                            v.wait_ge(S["scaled"], b + 1)
                            v.wait_ge(S["beta_added"], b + 1)
                            nc.vector.tensor_tensor(res[:, par], res[:, par], xin[:, par], ALU.add).then_inc(S["second_in"], 1)
                            v.wait_ge(S["second_in"], b + 1)
                            moments(b, par, 1, n)

                        def scales(b, r, n):
                            v.wait_ge(S[f"std{r + 1}"], b + 1)
                            nc.vector.reciprocal(scale_c[:, r, :, 2], scale_c[:, r, :, 1]).then_inc(S["inv_std"], 1)
                            v.wait_ge(S["inv_std"], n + 1)
                            nc.vector.scalar_tensor_tensor(out=scale_c[:, r, :, 3], in0=mom[:, r, :, 0], scalar=-1.0, in1=scale_c[:, r, :, 2],
                                                           op0=ALU.mult, op1=ALU.mult).then_inc(S[f"scale{r + 1}"], 1)

                        def turn(k, par, following=True, before=True, last=False, early=False):
                            if following:
                                messages(k + 1)
                            n = 2 * k - 1
                            residual(k, par, n if before else 0, last, early)
                            if before:
                                second(k - 1, 1 - par, n + 1)
                            scales(k, 0, n if before else 0)
                            if before:
                                scales(k - 1, 1, n + 1)

                        messages(0, first=True)
                        turn(0, 0, before=False, early=True)
                        turn(1, 1, early=True)
                        with v.Fori(1, PAIRS - 1) as i:
                            turn(2 * i, 0)
                            turn(2 * i + 1, 1)
                        turn(BATCHES - 2, 0)
                        if layer == 0:
                            nc.vector.memset(xin[:, 1, BATCH - 1], 0.0).then_inc(S["padded"], 1)
                        turn(BATCHES - 1, 1, following=False, last=True)
                        second(BATCHES - 1, 1, 2 * BATCHES - 1)
                        v.wait_ge(S["normed2"], (BATCHES - 1) * BATCH)
                        scales(BATCHES - 1, 1, 2 * BATCHES - 1)

        summing(0)
        node_stage(0)
        summing(1)
        node_stage(1)
    return nc


_INS = ['x', 'src', 'dst', 'edge_attr_3', 'edge_type_64', 'L0_gnn_query_emb', 'L0_gnn_Wq', 'L0_gnn_bq', 'L0_gnn_Wk',
        'L0_gnn_bk', 'L0_gnn_Wv', 'L0_gnn_bv', 'L0_gnn_rel_w', 'L0_gnn_Wo', 'L0_gnn_bo', 'L0_gnn_gamma', 'L0_gnn_beta',
        'L1_gnn_W1', 'L1_gnn_b1', 'L1_gnn_W2', 'L1_gnn_b2', 'L1_gnn_gamma', 'L1_gnn_beta']
_OUTS = [((N, D), 'float32')]


def kernel(**inputs):
    import numpy as _np
    import concourse.bacc as _bacc
    from concourse import mybir as _mybir
    from concourse.bass_utils import run_bass_kernel_spmd as _run

    nc = _bacc.Bacc("TRN2", target_bir_lowering=False, num_devices=1)
    arrays, args = {}, []
    for name in _INS:
        a = _np.ascontiguousarray(inputs[name])
        arrays[f"in_{name}_dram"] = a
        args.append(nc.dram_tensor(f"in_{name}_dram", a.shape, _mybir.dt.from_np(a.dtype), kind="ExternalInput").ap())
    for i, (shape, dtype) in enumerate(_OUTS):
        dt = _mybir.dt.from_np(_np.dtype(dtype))
        args.append(nc.dram_tensor(f"out_{i}_dram", shape, dt, kind="ExternalOutput").ap())
    gnn_kernel(nc, *args)
    r = _run(nc, [arrays], core_ids=[0])
    return r.results[0]["out_0_dram"]
```
